# Optimizing a Trainium2 kernel written in Bass

```python
import numpy as np
import jax
import jax.numpy as jnp

def _softmax(x, axis=-1):
    return jax.nn.softmax(x, axis=axis)

def _gelu(x):
    return jax.nn.gelu(x, approximate=True)

def _silu(x):
    return jax.nn.silu(x)

def _sigmoid(x):
    return jax.nn.sigmoid(x)

def _layernorm(x, axis=-1, eps=1e-05):
    m = jnp.mean(x, axis=axis, keepdims=True)
    v = jnp.var(x, axis=axis, keepdims=True)
    return (x - m) / jnp.sqrt(v + eps)

def _scatter_add(tgt, idx, src, axis=0):
    return tgt.at[idx].add(src)

def _segment_sum(src, seg, n):
    return jax.ops.segment_sum(src, seg, n)
kernel_name = 'mk_rec_standalone_d1_rec_r8_3e2244'

def setup_inputs(seed: int=0):
    np.random.seed(seed)
    _w = jnp.asarray

    def _rec_inputs():
        import jax
        import jax.numpy as jnp
        _rk = jax.random.key(seed)
        r_x = -0.000123307 + 1.00004 * jax.random.normal(jax.random.fold_in(_rk, 1), (512, 40, 128), jnp.float32)
        return r_x
    r_x = _rec_inputs()

    def _L0_rec_setup():
        import jax, jax.numpy as jnp
        import numpy as np
        NUM_FIELDS = 40
        EMB_DIM = 128
        BATCH = 256
        key = jax.random.key(seed)
        kx, kw = jax.random.split(key)
        x = jax.random.normal(kx, (BATCH, NUM_FIELDS, EMB_DIM), dtype=jnp.float32)
        W = jax.random.normal(kw, (EMB_DIM, EMB_DIM), dtype=jnp.float32) * np.float32(np.sqrt(1.0 / EMB_DIM))
        return {'x': x, 'W': W}
    _L0_rec_all = _L0_rec_setup()
    _L0_rec_in = {k: v for k, v in _L0_rec_all.items() if k in ('W',)}
    del _L0_rec_all
    return {'r_x': r_x, 'L0_rec_W': _L0_rec_in['W']}

def reference(r_x, L0_rec_W):
    import jax
    import jax.numpy as jnp

    def _L0_rec_ref(x, W):
        import jax, jax.numpy as jnp
        import numpy as np
        NUM_FIELDS = 40
        EMB_DIM = 128
        BATCH = 256
        vid = jnp.einsum('bfd,de->bfe', x, W)
        ii, jj = jnp.triu_indices(x.shape[1], k=1)
        return x[:, ii, :] * vid[:, jj, :]
    y = _L0_rec_ref(r_x, L0_rec_W)
    return y

_drawn_inputs = setup_inputs


def setup_inputs(seed=0):
    import zlib

    import numpy as np

    out = dict(_drawn_inputs(seed))
    spreads = {}
    factors = {}
    for name, (base, spread) in spreads.items():
        noise = np.random.default_rng([zlib.crc32(name.encode()), seed]).standard_normal(out[name].shape)
        drawn = base * np.exp(spread * noise) if base else spread * noise
        out[name] = jnp.asarray(drawn.astype(out[name].dtype))
    for name, factor in factors.items():
        out[name] = (out[name] * factor).astype(out[name].dtype)
    return out
```

```python
from contextlib import ExitStack

import concourse.bass as bass
from concourse import mybir

F32 = mybir.dt.float32
ALU = mybir.AluOpType
ACT = mybir.ActivationFunctionType


def pair_products_kernel(nc: bass.Bass, x: bass.AP, w: bass.AP, out: bass.AP):
    B, F, D = x.shape
    P = nc.NUM_PARTITIONS
    PAIRS = F * (F - 1) // 2
    TILES = B // P
    assert D == P and B % P == 0 and out.shape[1] == PAIRS

    GF = 512 // D
    GROUPS = F // GF
    GW = GF * D
    BUFS = 2
    assert F % GF == 0

    CP = F - 1
    CHUNKS = PAIRS // CP
    SLOTS = 4
    CW = CP * D
    assert PAIRS % CP == 0 and CHUNKS % SLOTS == 0

    PIECES = [(0, 0), (0, 1), (0, 3), (0, 6), (1, 0)]

    def cut_runs(step):
        runs, pair = [], 0
        for i in range(F - 1):
            j = i + 1
            while j < F:
                n = min(F - j, CP - pair % CP)
                if i == 0:
                    n = min(n, step - j % step)
                runs.append((pair // CP, pair % CP, i, j, n))
                pair += n
                j += n
        return runs

    x_tiles = x.rearrange("(t p) f d -> t p (f d)", p=P)
    out_tiles = out.rearrange("(t p) c d -> t p (c d)", p=P)

    with ExitStack() as ctx:
        def sb(name, shape):
            return ctx.enter_context(nc.sbuf_tensor(name, shape, F32))

        def psum(name, shape):
            return ctx.enter_context(nc.psum_tensor(name, shape, F32))

        def sem(name):
            return ctx.enter_context(nc.semaphore(name))

        xs = sb("xs", [P, 2 * F * D])
        vid = sb("vid", [P, 2 * F * D])
        prod = sb("prod", [P, SLOTS * CW])
        w_sb = sb("w_sb", [D, D])
        ident = sb("ident", [P, P])
        xT = sb("xT", [D, BUFS * GW])
        xT_ps = psum("xT_ps", [D, BUFS * GW])
        vid_ps = psum("vid_ps", [P, BUFS * GW])

        x_landed = {(half, k): sem(f"x_landed{half}_{k}") for half, k in PIECES}
        w_landed = sem("w_landed")
        ident_zeroed = sem("ident_zeroed")
        ident_ready = sem("ident_ready")
        transposed = sem("transposed")
        xT_ready = sem("xT_ready")
        projected = sem("projected")
        vid_ready = sem("vid_ready")
        chunk_ready = sem("chunk_ready")
        slot_stored = [sem(f"slot_stored{s}") for s in range(SLOTS)]

        block = ctx.enter_context(nc.Block())

        @block.gpsimd
        def _(pool):
            nc.gpsimd.memset(ident[:, :], 0.0).then_inc(ident_zeroed, 1)
            pool.wait_ge(ident_zeroed, 1)
            nc.gpsimd.affine_select(out=ident[:, :], in_=ident[:, :], compare_op=ALU.not_equal, fill=1.0,
                                    base=0, pattern=[[-1, P]], channel_multiplier=1).then_inc(ident_ready, 1)

        @block.tensor
        def _(pe):
            def transpose(g, g_half):
                buf = g_half % BUFS * GW
                for f in range(0, GW, D):
                    last = nc.tensor.transpose(xT_ps[:, buf + f:buf + f + D],
                                               xs[:, g_half * GW + f:g_half * GW + f + D], ident[:, :])
                last.then_inc(transposed, 1)

            def project(g, g_half):
                pe.wait_ge(xT_ready, g + 1)
                buf = g_half % BUFS * GW
                for f in range(0, GW, D):
                    last = nc.tensor.matmul(vid_ps[:, buf + f:buf + f + D], xT[:, buf + f:buf + f + D],
                                            w_sb[:, :], start=True, stop=True)
                last.then_inc(projected, 1)

            pe.wait_ge(ident_ready, 1)
            pe.wait_ge(w_landed, 16)
            with pe.Fori(0, TILES // 2) as u:
                for half in range(2):
                    g0 = (2 * u + half) * GROUPS
                    for k in range(GROUPS):
                        if (half, k) in x_landed:
                            pe.wait_ge(x_landed[half, k], 16 * (u + 1))
                        transpose(g0 + k, half * GROUPS + k)
                        if k > 0:
                            project(g0 + k - 1, half * GROUPS + k - 1)
                    project(g0 + GROUPS - 1, half * GROUPS + GROUPS - 1)

        @block.scalar
        def _(act):
            def load(t):
                for half, k in x_landed:
                    if half == t % 2:
                        end = min([c for h, c in x_landed if h == half and c > k] + [GROUPS])
                        act.dma_start(xs[:, (half * GROUPS + k) * GW:(half * GROUPS + end) * GW],
                                      x_tiles[t, :, k * GW:end * GW]).then_inc(x_landed[half, k], 16)

            def copy_xT(g):
                act.wait_ge(transposed, g + 1)
                buf = g % BUFS * GW
                nc.scalar.copy(xT[:, bass.ds(buf, GW)], xT_ps[:, bass.ds(buf, GW)]).then_inc(xT_ready, 1)

            def copy_vid(g):
                act.wait_ge(projected, g + 1)
                nc.scalar.copy(vid[:, bass.ds(g % (2 * GROUPS) * GW, GW)],
                               vid_ps[:, bass.ds(g % BUFS * GW, GW)]).then_inc(vid_ready, 1)

            load(0)
            load(1)
            for t in range(TILES):
                if t >= 2:
                    act.wait_ge(chunk_ready, (t - 1) * CHUNKS)
                    load(t)
                copy_xT(t * GROUPS)
                with act.Fori(t * GROUPS, (t + 1) * GROUPS - 1) as g:
                    copy_xT(g + 1)
                    copy_vid(g)
                copy_vid((t + 1) * GROUPS - 1)

        @block.vector
        def _(dve):
            def multiply_tile(t, runs):
                half = t % 2 * (F * D)
                for chunk, at, i, j, n in runs:
                    slot = chunk % SLOTS
                    used = t * (CHUNKS // SLOTS) + chunk // SLOTS
                    if at == 0 and not (isinstance(used, int) and used == 0):
                        dve.wait_ge(slot_stored[slot], 16 * used)
                    if i == 0:
                        dve.wait_ge(vid_ready, t * GROUPS + -(-(j + n) // GF))
                    lo = slot * CW + at * D
                    o = prod[:, lo:lo + n * D].rearrange("p (n d) -> p n d", d=D)
                    xi = xs[:, bass.ds(half + i * D, D)].unsqueeze(1).to_broadcast([P, n, D])
                    vj = vid[:, bass.ds(half + j * D, n * D)].rearrange("p (n d) -> p n d", d=D)
                    made = nc.vector.tensor_tensor(out=o, in0=xi, in1=vj, op=ALU.mult)
                    if at + n == CP:
                        made.then_inc(chunk_ready, 1)

            multiply_tile(0, cut_runs(2 * GF))
            with dve.Fori(1, TILES) as t:
                multiply_tile(t, cut_runs(F))

        @block.sync
        def _(sp):
            sp.dma_start(w_sb[:, :], w).then_inc(w_landed, 16)
            with sp.Fori(0, TILES) as t:
                for chunk in range(CHUNKS):
                    slot = chunk % SLOTS
                    sp.wait_ge(chunk_ready, t * CHUNKS + chunk + 1)
                    sp.dma_start(out_tiles[bass.ds(t, 1), :, chunk * CW:(chunk + 1) * CW],
                                 prod[:, slot * CW:(slot + 1) * CW]).then_inc(slot_stored[slot], 16)
            for stored in slot_stored:
                sp.wait_ge(stored, 16 * TILES * CHUNKS // SLOTS)

    return nc


def kernel(**inputs):
    import numpy as _np
    import concourse.bacc as _bacc
    from concourse import mybir as _mybir
    from concourse.bass_utils import run_bass_kernel_spmd as _run

    nc = _bacc.Bacc("TRN2", target_bir_lowering=False, num_devices=1)
    x = _np.ascontiguousarray(inputs["r_x"])
    w = _np.ascontiguousarray(inputs["L0_rec_W"])
    b, f, d = x.shape
    arrays = {"x_dram": x, "w_dram": w}
    args = [nc.dram_tensor(name, a.shape, _mybir.dt.from_np(a.dtype), kind="ExternalInput").ap()
            for name, a in arrays.items()]
    out = nc.dram_tensor("out_dram", (b, f * (f - 1) // 2, d), _mybir.dt.float32, kind="ExternalOutput").ap()
    pair_products_kernel(nc, *args, out)
    r = _run(nc, [arrays], core_ids=[0])
    return r.results[0]["out_dram"]
```

```python
from contextlib import ExitStack

import concourse.bass as bass
from concourse import mybir

F32 = mybir.dt.float32
ALU = mybir.AluOpType
ACT = mybir.ActivationFunctionType


def pair_products_kernel(nc: bass.Bass, x: bass.AP, w: bass.AP, out: bass.AP):
    B, F, D = x.shape
    P = nc.NUM_PARTITIONS
    PAIRS = F * (F - 1) // 2
    TILES = B // P
    assert D == P and B % P == 0 and out.shape[1] == PAIRS

    GF = 512 // D
    GROUPS = F // GF
    GW = GF * D
    BUFS = 2
    assert F % GF == 0

    CP = F - 1
    CHUNKS = PAIRS // CP
    SLOTS = 5
    CW = CP * D
    assert PAIRS % CP == 0 and CHUNKS % SLOTS == 0

    PIECES = [(0, 0), (0, 2), (0, 5), (1, 0)]

    def first_pair(i, j):
        return i * F - i * (i + 1) // 2 + j - i - 1

    def rows_from(first_i):
        stores, room = [], 0
        for i in range(first_i, F - 1):
            j = i + 1
            while j < F:
                if room == 0:
                    stores.append([])
                    room = CP
                n = min(F - j, room)
                stores[-1].append((i, j, n))
                j += n
                room -= n
        return stores

    NEAR = 3 * GF
    first_stores = ([[(i, i + 1, NEAR - 1 - i)] for i in range(NEAR - 1)]
                    + [[(i, NEAR, F - NEAR)] for i in range(NEAR - 1)]
                    + rows_from(NEAR - 1))
    later_stores = rows_from(0)
    assert len(later_stores) == CHUNKS

    first_places, stores_of_slot, fill, at = [], [0] * SLOTS, 0, 0
    for store in first_stores:
        n = sum(n for _, _, n in store)
        if at + n > CP:
            fill, at = fill + 1, 0
        if at == 0:
            stored_before = stores_of_slot[fill % SLOTS]
        first_places.append((fill % SLOTS, at, stored_before))
        stores_of_slot[fill % SLOTS] += 1
        at += n
    first_fills = fill + 1

    def places(t):
        for c in range(CHUNKS):
            slot = (first_fills + c) % SLOTS
            yield slot, 0, stores_of_slot[slot] + (t - 1) * (CHUNKS // SLOTS) + c // SLOTS

    x_tiles = x.rearrange("(t p) f d -> t p (f d)", p=P)
    out_tiles = out.rearrange("(t p) c d -> t p (c d)", p=P)

    with ExitStack() as ctx:
        def sb(name, shape):
            return ctx.enter_context(nc.sbuf_tensor(name, shape, F32))

        def psum(name, shape):
            return ctx.enter_context(nc.psum_tensor(name, shape, F32))

        def sem(name):
            return ctx.enter_context(nc.semaphore(name))

        xs = sb("xs", [P, 2 * F * D])
        vid = sb("vid", [P, 2 * F * D])
        prod = sb("prod", [P, SLOTS * CW])
        w_sb = sb("w_sb", [D, D])
        ident = sb("ident", [P, P])
        xT = sb("xT", [D, BUFS * GW])
        xT_ps = psum("xT_ps", [D, BUFS * GW])
        vid_ps = psum("vid_ps", [P, BUFS * GW])

        x_landed = {(half, k): sem(f"x_landed{half}_{k}") for half, k in PIECES}
        w_landed = sem("w_landed")
        ident_zeroed = sem("ident_zeroed")
        ident_ready = sem("ident_ready")
        transposed = sem("transposed")
        xT_ready = sem("xT_ready")
        projected = sem("projected")
        vid_ready = sem("vid_ready")
        store_ready = sem("store_ready")
        slot_stored = [sem(f"slot_stored{s}") for s in range(SLOTS)]

        block = ctx.enter_context(nc.Block())

        @block.gpsimd
        def _(pool):
            nc.gpsimd.memset(ident[:, :], 0.0).then_inc(ident_zeroed, 1)
            pool.wait_ge(ident_zeroed, 1)
            nc.gpsimd.affine_select(out=ident[:, :], in_=ident[:, :], compare_op=ALU.not_equal, fill=1.0,
                                    base=0, pattern=[[-1, P]], channel_multiplier=1).then_inc(ident_ready, 1)

        @block.tensor
        def _(pe):
            def transpose(g, g_half):
                buf = g_half % BUFS * GW
                for f in range(0, GW, D):
                    last = nc.tensor.transpose(xT_ps[:, buf + f:buf + f + D],
                                               xs[:, g_half * GW + f:g_half * GW + f + D], ident[:, :])
                last.then_inc(transposed, 1)

            def project(g, g_half):
                pe.wait_ge(xT_ready, g + 1)
                buf = g_half % BUFS * GW
                for f in range(0, GW, D):
                    last = nc.tensor.matmul(vid_ps[:, buf + f:buf + f + D], xT[:, buf + f:buf + f + D],
                                            w_sb[:, :], start=True, stop=True)
                last.then_inc(projected, 1)

            pe.wait_ge(ident_ready, 1)
            pe.wait_ge(w_landed, 16)
            with pe.Fori(0, TILES // 2) as u:
                for half in range(2):
                    g0 = (2 * u + half) * GROUPS
                    for k in range(GROUPS):
                        if (half, k) in x_landed:
                            pe.wait_ge(x_landed[half, k], 16 * (u + 1))
                        transpose(g0 + k, half * GROUPS + k)
                        if k > 0:
                            project(g0 + k - 1, half * GROUPS + k - 1)
                    project(g0 + GROUPS - 1, half * GROUPS + GROUPS - 1)

        @block.scalar
        def _(act):
            def load(t):
                for half, k in x_landed:
                    if half == t % 2:
                        end = min([c for h, c in x_landed if h == half and c > k] + [GROUPS])
                        act.dma_start(xs[:, (half * GROUPS + k) * GW:(half * GROUPS + end) * GW],
                                      x_tiles[t, :, k * GW:end * GW]).then_inc(x_landed[half, k], 16)
                        if (t, k) == (0, 0):
                            act.dma_start(w_sb[:, :], w).then_inc(w_landed, 16)

            def copy_xT(g):
                act.wait_ge(transposed, g + 1)
                buf = g % BUFS * GW
                nc.scalar.copy(xT[:, bass.ds(buf, GW)], xT_ps[:, bass.ds(buf, GW)]).then_inc(xT_ready, 1)

            def copy_vid(g):
                act.wait_ge(projected, g + 1)
                nc.scalar.copy(vid[:, bass.ds(g % (2 * GROUPS) * GW, GW)],
                               vid_ps[:, bass.ds(g % BUFS * GW, GW)]).then_inc(vid_ready, 1)

            load(0)
            load(1)
            for t in range(TILES):
                if t >= 2:
                    act.wait_ge(store_ready, len(first_stores) + (t - 2) * CHUNKS)
                    load(t)
                copy_xT(t * GROUPS)
                with act.Fori(t * GROUPS, (t + 1) * GROUPS - 1) as g:
                    copy_xT(g + 1)
                    copy_vid(g)
                copy_vid((t + 1) * GROUPS - 1)

        @block.vector
        def _(dve):
            def multiply(t, store, slot, at):
                half = t % 2 * (F * D)
                lo = slot * CW + at * D
                for i, j, n in store:
                    xi = xs[:, bass.ds(half + i * D, D)].unsqueeze(1).to_broadcast([P, n, D])
                    vj = vid[:, bass.ds(half + j * D, n * D)].rearrange("p (n d) -> p n d", d=D)
                    o = prod[:, lo:lo + n * D].rearrange("p (n d) -> p n d", d=D)
                    made = nc.vector.tensor_tensor(out=o, in0=xi, in1=vj, op=ALU.mult)
                    lo += n * D
                made.then_inc(store_ready, 1)

            seen = 0
            for store, (slot, at, stored_before) in zip(first_stores, first_places):
                need = -(-max(j + n for _, j, n in store) // GF)
                if need > seen:
                    dve.wait_ge(vid_ready, need)
                    seen = need
                if at == 0 and stored_before > 0:
                    dve.wait_ge(slot_stored[slot], 16 * stored_before)
                multiply(0, store, slot, at)
            with dve.Fori(1, TILES) as t:
                dve.wait_ge(vid_ready, (t + 1) * GROUPS)
                for store, (slot, at, stored_before) in zip(later_stores, places(t)):
                    dve.wait_ge(slot_stored[slot], 16 * stored_before)
                    multiply(t, store, slot, at)

        @block.sync
        def _(sp):
            def put(t, store, slot, at):
                lo = first_pair(*store[0][:2])
                n = sum(n for _, _, n in store)
                sp.dma_start(out_tiles[bass.ds(t, 1), :, lo * D:(lo + n) * D],
                             prod[:, slot * CW + at * D:slot * CW + (at + n) * D]).then_inc(slot_stored[slot], 16)

            for s, (store, (slot, at, _)) in enumerate(zip(first_stores, first_places)):
                sp.wait_ge(store_ready, s + 1)
                put(0, store, slot, at)
            with sp.Fori(1, TILES) as t:
                for c, (store, (slot, at, _)) in enumerate(zip(later_stores, places(t))):
                    sp.wait_ge(store_ready, len(first_stores) + (t - 1) * CHUNKS + c + 1)
                    put(t, store, slot, at)
            for slot, _, stored in list(places(TILES))[:SLOTS]:
                sp.wait_ge(slot_stored[slot], 16 * stored)

    return nc


def kernel(**inputs):
    import numpy as _np
    import concourse.bacc as _bacc
    from concourse import mybir as _mybir
    from concourse.bass_utils import run_bass_kernel_spmd as _run

    nc = _bacc.Bacc("TRN2", target_bir_lowering=False, num_devices=1)
    x = _np.ascontiguousarray(inputs["r_x"])
    w = _np.ascontiguousarray(inputs["L0_rec_W"])
    b, f, d = x.shape
    arrays = {"x_dram": x, "w_dram": w}
    args = [nc.dram_tensor(name, a.shape, _mybir.dt.from_np(a.dtype), kind="ExternalInput").ap()
            for name, a in arrays.items()]
    out = nc.dram_tensor("out_dram", (b, f * (f - 1) // 2, d), _mybir.dt.float32, kind="ExternalOutput").ap()
    pair_products_kernel(nc, *args, out)
    r = _run(nc, [arrays], core_ids=[0])
    return r.results[0]["out_dram"]
```
